# Optimizing a Trainium2 kernel written in Bass

```python
import numpy as np
import jax
import jax.numpy as jnp

def _softmax(x, axis=-1):
    return jax.nn.softmax(x, axis=axis)

def _gelu(x):
    return jax.nn.gelu(x, approximate=True)

def _silu(x):
    return jax.nn.silu(x)

def _sigmoid(x):
    return jax.nn.sigmoid(x)

def _layernorm(x, axis=-1, eps=1e-05):
    m = jnp.mean(x, axis=axis, keepdims=True)
    v = jnp.var(x, axis=axis, keepdims=True)
    return (x - m) / jnp.sqrt(v + eps)

def _scatter_add(tgt, idx, src, axis=0):
    return tgt.at[idx].add(src)

def _segment_sum(src, seg, n):
    return jax.ops.segment_sum(src, seg, n)
kernel_name = 'mk_rec_standalone_d1_rec_r8_40817f'

def setup_inputs(seed: int=0):
    np.random.seed(seed)
    _w = jnp.asarray

    def _rec_inputs():
        import jax
        import jax.numpy as jnp
        _rk = jax.random.key(seed)
        r_x = -7.10856e-05 + 0.999911 * jax.random.normal(jax.random.fold_in(_rk, 1), (2048, 512, 64), jnp.float32)
        return r_x
    r_x = _rec_inputs()

    def _L0_rec_setup():
        import jax, jax.numpy as jnp
        import numpy as np
        B, DIM, C = (256, 512, 64)
        INTER = DIM // 4
        EPS = 1e-05
        key = jax.random.key(seed)
        ks = jax.random.split(key, 14)

        def n(k, shape, scale=0.05):
            return jax.random.normal(k, shape, dtype=jnp.float32) * scale
        return {'x': jax.random.normal(ks[0], (B, DIM, C), dtype=jnp.float32), 'W1': n(ks[1], (C, INTER, DIM)), 'b1': n(ks[2], (C, INTER)), 'g1': 1.0 + n(ks[3], (C, INTER)), 'be1': n(ks[4], (C, INTER)), 'm1': n(ks[5], (C, INTER)), 'v1': jax.random.uniform(ks[6], (C, INTER), dtype=jnp.float32, minval=0.5, maxval=1.5), 'W2': n(ks[7], (C, DIM, INTER)), 'b2': n(ks[8], (C, DIM)), 'g2': 1.0 + n(ks[9], (C, DIM)), 'be2': n(ks[10], (C, DIM)), 'm2': n(ks[11], (C, DIM)), 'v2': jax.random.uniform(ks[12], (C, DIM), dtype=jnp.float32, minval=0.5, maxval=1.5)}
    _L0_rec_all = _L0_rec_setup()
    _L0_rec_in = {k: v for k, v in _L0_rec_all.items() if k in ('W1', 'b1', 'g1', 'be1', 'm1', 'v1', 'W2', 'b2', 'g2', 'be2', 'm2', 'v2')}
    del _L0_rec_all
    return {'r_x': r_x, 'L0_rec_W1': _L0_rec_in['W1'], 'L0_rec_b1': _L0_rec_in['b1'], 'L0_rec_g1': _L0_rec_in['g1'], 'L0_rec_be1': _L0_rec_in['be1'], 'L0_rec_m1': _L0_rec_in['m1'], 'L0_rec_v1': _L0_rec_in['v1'], 'L0_rec_W2': _L0_rec_in['W2'], 'L0_rec_b2': _L0_rec_in['b2'], 'L0_rec_g2': _L0_rec_in['g2'], 'L0_rec_be2': _L0_rec_in['be2'], 'L0_rec_m2': _L0_rec_in['m2'], 'L0_rec_v2': _L0_rec_in['v2']}

def reference(r_x, L0_rec_W1, L0_rec_b1, L0_rec_g1, L0_rec_be1, L0_rec_m1, L0_rec_v1, L0_rec_W2, L0_rec_b2, L0_rec_g2, L0_rec_be2, L0_rec_m2, L0_rec_v2):
    import jax
    import jax.numpy as jnp

    def _L0_rec_ref(x, W1, b1, g1, be1, m1, v1, W2, b2, g2, be2, m2, v2):
        import jax, jax.numpy as jnp
        import numpy as np
        B, DIM, C = (256, 512, 64)
        INTER = DIM // 4
        EPS = 1e-05
        h = jnp.einsum('bdc,cid->bci', x, W1) + b1[None]
        h = (h - m1[None]) * (g1[None] * jax.lax.rsqrt(v1 + EPS)[None]) + be1[None]
        h = jax.nn.relu(h)
        y = jnp.einsum('bci,cdi->bcd', h, W2) + b2[None]
        y = (y - m2[None]) * (g2[None] * jax.lax.rsqrt(v2 + EPS)[None]) + be2[None]
        w = jax.nn.sigmoid(jnp.transpose(y, (0, 2, 1)))
        return w
    y = _L0_rec_ref(r_x, L0_rec_W1, L0_rec_b1, L0_rec_g1, L0_rec_be1, L0_rec_m1, L0_rec_v1, L0_rec_W2, L0_rec_b2, L0_rec_g2, L0_rec_be2, L0_rec_m2, L0_rec_v2)
    return y

_drawn_inputs = setup_inputs


def setup_inputs(seed=0):
    import zlib

    import numpy as np

    out = dict(_drawn_inputs(seed))
    spreads = {}
    factors = {'L0_rec_b1': 5.655,
     'L0_rec_g1': 4.964,
     'L0_rec_be1': 5.901,
     'L0_rec_m1': 5.695,
     'L0_rec_g2': 200.0,
     'L0_rec_be2': 24.283,
     'L0_rec_v2': 21.806}
    for name, (base, spread) in spreads.items():
        noise = np.random.default_rng([zlib.crc32(name.encode()), seed]).standard_normal(out[name].shape)
        drawn = base * np.exp(spread * noise) if base else spread * noise
        out[name] = jnp.asarray(drawn.astype(out[name].dtype))
    for name, factor in factors.items():
        out[name] = (out[name] * factor).astype(out[name].dtype)
    return out
```

```python
from contextlib import ExitStack

import concourse.bass as bass
from concourse import mybir

P = 128
F32 = mybir.dt.float32
F32R = mybir.dt.float32r
ALU = mybir.AluOpType
ACT_FN = mybir.ActivationFunctionType
EPS = 1e-5

NB = 512
X_SLOTS = 4
H_SLOTS = 2
W_SLOTS = 2
CH_PER_BODY = 2
LOAD_LEAD = 6
SPLIT_LEAD = 3
HALVES = 2
DMA = 16
KINDS = 5


def build(nc, x, weights, params, out, channels, dim, inter, blocks):
    J = dim // P
    Q = blocks
    UNITS = channels * Q
    U_BODY = CH_PER_BODY * Q
    BODIES = channels // CH_PER_BODY
    FW = J * inter
    GROUPS = 1 + J
    assert inter == P and U_BODY % X_SLOTS == 0 and U_BODY % H_SLOTS == 0
    assert CH_PER_BODY == W_SLOTS and BODIES >= 3

    with ExitStack() as ctx:
        def sb(name, shape, dt=F32):
            return ctx.enter_context(nc.sbuf_tensor(name, shape, dt))

        def sem(name):
            return ctx.enter_context(nc.semaphore(name))

        x_raw = sb("x_raw", [P, X_SLOTS, J * NB])
        x_hi = sb("x_hi", [P, X_SLOTS, J * NB], F32R)
        x_lo = sb("x_lo", [P, X_SLOTS, J * NB], F32R)
        w_raw = sb("w_raw", [P, W_SLOTS, 2 * FW])
        w_hi = sb("w_hi", [P, W_SLOTS, 2 * FW], F32R)
        w_lo = sb("w_lo", [P, W_SLOTS, 2 * FW], F32R)
        h_raw = sb("h_raw", [P, H_SLOTS, NB])
        h_hi = sb("h_hi", [P, H_SLOTS, NB], F32R)
        h_lo = sb("h_lo", [P, H_SLOTS, NB], F32R)
        y_out = sb("y_out", [P, X_SLOTS, J * NB])

        par = sb("par", [P, KINDS, channels, GROUPS])
        veps = sb("veps", [P, channels, GROUPS])
        root = sb("root", [P, channels, GROUPS])
        rinv = sb("rinv", [P, channels, GROUPS])
        fix = sb("fix", [P, channels, GROUPS])
        norms = sb("norms", [P, channels, 2, GROUPS])
        norm_now = sb("norm_now", [P, W_SLOTS, 2, GROUPS])

        h_psum = ctx.enter_context(nc.psum_tensor("h_psum", [P, H_SLOTS, NB], F32))
        y_psum = ctx.enter_context(nc.psum_tensor("y_psum", [P, J, NB], F32))

        x_loaded = [sem(f"x_loaded{s}") for s in range(X_SLOTS)]
        w_loaded = [sem(f"w_loaded{s}") for s in range(W_SLOTS)]
        out_stored = [sem(f"out_stored{s}") for s in range(X_SLOTS)]
        par_loaded = sem("par_loaded")
        par_step = sem("par_step")
        root_done = sem("root_done")
        norms_set = sem("norms_set")
        w_hi_done = sem("w_hi_done")
        w_split = sem("w_split")
        x_hi_done = sem("x_hi_done")
        x_split = sem("x_split")
        h_hi_done = sem("h_hi_done")
        h_split = sem("h_split")
        layer1_done = sem("layer1_done")
        h_done = sem("h_done")
        layer2_done = sem("layer2_done")
        y_done = sem("y_done")

        block = ctx.enter_context(nc.Block())

        def bodies(engine, body):
            body(0, first=True)
            with engine.Fori(1, BODIES - 1) as g:
                body(g)
            body(BODIES - 1, last=True)

        @block.sync
        def _(sp):
            def load_weights(channel, slot):
                sp.dma_start(w_raw[:, slot, :], weights[channel, :, :]).then_inc(w_loaded[slot], DMA)

            def load_x(unit, slot):
                sp.dma_start(x_raw[:, slot, :], x[unit, :, :]).then_inc(x_loaded[slot], DMA)

            def body(g, first=False, last=False):
                for k in range(U_BODY):
                    if not (last and k + LOAD_LEAD >= U_BODY):
                        unit = U_BODY * g + k + LOAD_LEAD
                        sp.wait_ge(x_split, HALVES * (unit - X_SLOTS + 1))
                        load_x(unit, (k + LOAD_LEAD) % X_SLOTS)
                    if k % Q == 0 and not last:
                        slot = k // Q
                        sp.wait_ge(w_split, CH_PER_BODY * g + slot + 1)
                        load_weights(CH_PER_BODY * g + slot + W_SLOTS, slot)
                    unit, slot = U_BODY * g + k, k % X_SLOTS
                    if last and k == U_BODY - 1:
                        for j in range(J):
                            cols = slice(j * NB, (j + 1) * NB)
                            sp.wait_ge(y_done, J * unit + j + 1)
                            sp.dma_start(out[unit, :, cols], y_out[:, slot, cols])\
                                .then_inc(out_stored[slot], DMA)
                    else:
                        sp.wait_ge(y_done, J * (unit + 1))
                        sp.dma_start(out[unit, :, :], y_out[:, slot, :]).then_inc(out_stored[slot], DMA)

            load_weights(0, 0)
            load_x(0, 0)
            sp.dma_start(par[:, :, :, :], params).then_inc(par_loaded, DMA)
            load_x(1, 1)
            load_weights(1, 1)
            for u in range(2, LOAD_LEAD):
                if u >= X_SLOTS:
                    sp.wait_ge(x_split, HALVES * (u - X_SLOTS + 1))
                load_x(u, u % X_SLOTS)
            bodies(sp, body)
            for s in range(X_SLOTS):
                stores = UNITS // X_SLOTS + (J - 1 if s == X_SLOTS - 1 else 0)
                sp.wait_ge(out_stored[s], DMA * stores)

        @block.vector
        def _(dve):
            def split_weights(channel, slot, fill, free):
                dve.wait_ge(w_loaded[slot], DMA * fill)
                if free is not None:
                    dve.wait_ge(y_done, free)
                dve.tensor_copy(w_hi[:, slot, :], w_raw[:, slot, :]).then_inc(w_hi_done, 1)
                dve.wait_ge(w_hi_done, channel + 1)
                dve.tensor_tensor(w_lo[:, slot, :], w_raw[:, slot, :], w_hi[:, slot, :].bitcast(F32),
                                  ALU.subtract).then_inc(w_split, 1)

            def set_norm(channel, slot):
                dve.tensor_copy(norm_now[:, slot, :, :], norms[:, bass.ds(channel, 1), :, :])\
                   .then_inc(norms_set, 1)

            def split_x(unit, slot, fill, free):
                dve.wait_ge(x_loaded[slot], DMA * fill)
                if free is not None:
                    dve.wait_ge(layer1_done, free)
                for half in range(HALVES):
                    cols = slice(half * J * NB // HALVES, (half + 1) * J * NB // HALVES)
                    dve.tensor_copy(x_hi[:, slot, cols], x_raw[:, slot, cols]).then_inc(x_hi_done, 1)
                    dve.wait_ge(x_hi_done, HALVES * unit + half + 1)
                    dve.tensor_tensor(x_lo[:, slot, cols], x_raw[:, slot, cols],
                                      x_hi[:, slot, cols].bitcast(F32), ALU.subtract).then_inc(x_split, 1)

            def split_h(unit, slot, free):
                dve.wait_ge(h_done, unit + 1)
                if free is not None:
                    dve.wait_ge(layer2_done, free)
                dve.tensor_copy(h_hi[:, slot, :], h_raw[:, slot, :]).then_inc(h_hi_done, 1)
                dve.wait_ge(h_hi_done, unit + 1)
                dve.tensor_tensor(h_lo[:, slot, :], h_raw[:, slot, :], h_hi[:, slot, :].bitcast(F32),
                                  ALU.subtract).then_inc(h_split, 1)

            steps = [0]

            def step(instruction):
                steps[0] += 1
                instruction.then_inc(par_step, 1)
                dve.wait_ge(par_step, steps[0])

            def norm_parameters():
                b, gamma, beta, mean, var = (par[:, n, :, :] for n in range(KINDS))
                scale, bias = (norms[:, :, n, :] for n in range(2))
                dve.wait_ge(par_loaded, DMA)
                step(dve.tensor_scalar(veps[:, :, :], var, EPS, None, ALU.add))
                dve.wait_ge(root_done, 1)
                step(dve.reciprocal(rinv[:, :, :], root[:, :, :]))
                step(dve.tensor_tensor(fix[:, :, :], rinv[:, :, :], rinv[:, :, :], ALU.mult))
                step(dve.tensor_tensor(fix[:, :, :], fix[:, :, :], veps[:, :, :], ALU.mult))
                step(dve.tensor_scalar(fix[:, :, :], fix[:, :, :], -0.5, 1.5, ALU.mult, ALU.add))
                step(dve.tensor_tensor(rinv[:, :, :], rinv[:, :, :], fix[:, :, :], ALU.mult))
                step(dve.tensor_tensor(scale, gamma, rinv[:, :, :], ALU.mult))
                step(dve.tensor_tensor(bias, b, mean, ALU.subtract))
                step(dve.tensor_tensor(bias, bias, scale, ALU.mult))
                step(dve.tensor_tensor(bias, bias, beta, ALU.add))

            def body(g, first=False, last=False):
                for k in range(U_BODY):
                    if not (last and k + 1 == U_BODY):
                        unit, slot = U_BODY * g + k + 1, (k + 1) % H_SLOTS
                        split_h(unit, slot, None if first and k + 1 < H_SLOTS else J * (unit - H_SLOTS + 1))
                    n = k + SPLIT_LEAD
                    if last and n >= U_BODY - 1:
                        n -= 1
                    if not (last and (k == U_BODY - SPLIT_LEAD - 1 or n >= U_BODY)):
                        unit = U_BODY * g + n
                        split_x(unit, n % X_SLOTS, U_BODY // X_SLOTS * g + n // X_SLOTS + 1,
                                None if first and n < X_SLOTS else unit - X_SLOTS + 1)
                    if k % Q == 1 and not (last and k > Q):
                        n = k // Q + 1
                        slot = n % W_SLOTS
                        channel = CH_PER_BODY * g + n
                        split_weights(channel, slot, g + n // W_SLOTS + 1,
                                      None if first and n < W_SLOTS else J * Q * (channel - W_SLOTS + 1))
                        set_norm(channel, slot)

            split_weights(0, 0, 1, None)
            split_x(0, 0, 1, None)
            norm_parameters()
            set_norm(0, 0)
            split_x(1, 1, 1, None)
            split_h(0, 0, None)
            split_x(2, 2, 1, None)
            bodies(dve, body)

        @block.tensor
        def _(pe):
            def three_passes(acc, w, x_parts, first, last):
                (wh, wl), (xh, xl) = w, x_parts
                pe.matmul(acc, wh, xh, start=first, stop=False)
                pe.matmul(acc, wh, xl, start=False, stop=False)
                return pe.matmul(acc, wl, xh, start=False, stop=last)

            def layer1(unit, k, channel, w_slot, free):
                if k % Q == 0:
                    pe.wait_ge(w_split, channel + 1)
                if free is not None:
                    pe.wait_ge(h_done, free)
                for j in range(J):
                    if j % (J // HALVES) == 0:
                        pe.wait_ge(x_split, HALVES * unit + j // (J // HALVES) + 1)
                    cols, rows = slice(j * NB, (j + 1) * NB), slice(j * inter, (j + 1) * inter)
                    mm = three_passes(h_psum[:, k % H_SLOTS, :],
                                      (w_hi[:, w_slot, rows], w_lo[:, w_slot, rows]),
                                      (x_hi[:, k % X_SLOTS, cols], x_lo[:, k % X_SLOTS, cols]),
                                      j == 0, j == J - 1)
                mm.then_inc(layer1_done, 1)

            def layer2(unit, k, w_slot, first):
                pe.wait_ge(h_split, unit + 1)
                for j in range(J):
                    if not first:
                        pe.wait_ge(y_done, J * (unit - 1) + j + 1)
                    rows = slice(FW + j * P, FW + (j + 1) * P)
                    three_passes(y_psum[:, j, :],
                                 (w_hi[:, w_slot, rows], w_lo[:, w_slot, rows]),
                                 (h_hi[:, k % H_SLOTS, :], h_lo[:, k % H_SLOTS, :]),
                                 True, True).then_inc(layer2_done, 1)

            def body(g, first=False, last=False):
                for k in range(U_BODY):
                    n = k + 1
                    if not (last and n == U_BODY):
                        unit = U_BODY * g + n
                        layer1(unit, n, CH_PER_BODY * g + n // Q, n // Q % W_SLOTS,
                               None if first and n < H_SLOTS else unit - H_SLOTS + 1)
                    layer2(U_BODY * g + k, k, k // Q, first and k == 0)

            layer1(0, 0, 0, 0, None)
            bodies(pe, body)

        @block.scalar
        def _(act):
            def norm(group, w_slot):
                return dict(scale=norm_now[:, w_slot, 0, group:group + 1],
                            bias=norm_now[:, w_slot, 1, group:group + 1])

            def finish_h(unit, k, channel, free):
                slot, w_slot = k % H_SLOTS, k // Q % W_SLOTS
                if k % Q == 0:
                    act.wait_ge(norms_set, channel + 1)
                act.wait_ge(layer1_done, unit + 1)
                if free is not None:
                    act.wait_ge(h_split, free)
                act.activation(h_raw[:, slot, :], h_psum[:, slot, :], ACT_FN.Relu,
                               **norm(0, w_slot)).then_inc(h_done, 1)

            def finish_y(unit, k, stored):
                slot, w_slot = k % X_SLOTS, k // Q % W_SLOTS
                if stored is not None:
                    act.wait_ge(out_stored[slot], stored)
                for j in range(J):
                    act.wait_ge(layer2_done, J * unit + j + 1)
                    act.activation(y_out[:, slot, j * NB:(j + 1) * NB], y_psum[:, j, :], ACT_FN.Sigmoid,
                                   **norm(1 + j, w_slot)).then_inc(y_done, 1)

            def body(g, first=False, last=False):
                for k in range(U_BODY):
                    n = k + 1
                    if not (last and n == U_BODY):
                        unit = U_BODY * g + n
                        finish_h(unit, n, CH_PER_BODY * g + n // Q,
                                 None if first and n < H_SLOTS else unit - H_SLOTS + 1)
                    finish_y(U_BODY * g + k, k,
                             None if first and k < X_SLOTS else
                             DMA * (U_BODY // X_SLOTS * g + k // X_SLOTS))

            act.wait_ge(par_step, 1)
            act.activation(root[:, :, :], veps[:, :, :], ACT_FN.Sqrt).then_inc(root_done, 1)
            finish_h(0, 0, 0, None)
            bodies(act, body)


def kernel(r_x, **w):
    import numpy as np
    import concourse.bacc as bacc
    from concourse.bass_utils import run_bass_kernel_spmd

    L = {k[len("L0_rec_"):]: np.asarray(v) for k, v in w.items()}
    x = np.asarray(r_x)
    batch, dim, channels = x.shape
    inter = L["W1"].shape[1]
    J, Q = dim // P, batch // NB

    x_t = np.ascontiguousarray(x.reshape(Q, NB, P, J, channels).transpose(4, 0, 2, 3, 1))
    x_t = x_t.reshape(channels * Q, P, J * NB)
    w1 = L["W1"].reshape(channels, inter, P, J).transpose(0, 2, 3, 1).reshape(channels, P, J * inter)
    w2 = L["W2"].reshape(channels, P, J, inter).transpose(0, 3, 2, 1).reshape(channels, inter, J * P)
    weights = np.concatenate([w1, w2], axis=2)
    rows = []
    for kind in ("b", "g", "be", "m", "v"):
        first = L[kind + "1"].T[:, :, None]
        second = L[kind + "2"].reshape(channels, P, J).transpose(1, 0, 2)
        rows.append(np.concatenate([first, second], axis=2))
    params = np.stack(rows, axis=1)

    nc = bacc.Bacc("TRN2", target_bir_lowering=False, num_devices=1)
    arrays = {"x": x_t, "weights": np.ascontiguousarray(weights), "params": np.ascontiguousarray(params)}
    args = [nc.dram_tensor(n, a.shape, mybir.dt.from_np(a.dtype), kind="ExternalInput").ap()
            for n, a in arrays.items()]
    out = nc.dram_tensor("out", x_t.shape, F32, kind="ExternalOutput").ap()
    build(nc, *args, out, channels, dim, inter, Q)
    r = run_bass_kernel_spmd(nc, [arrays], core_ids=[0])
    y = np.asarray(r.results[0]["out"]).reshape(channels, Q, P, J, NB)
    return np.ascontiguousarray(y.transpose(1, 4, 2, 3, 0)).reshape(batch, dim, channels)
```
